# Optimizing a Trainium2 kernel written in Bass

```python
import numpy as np
import jax
import jax.numpy as jnp

def _softmax(x, axis=-1):
    return jax.nn.softmax(x, axis=axis)

def _gelu(x):
    return jax.nn.gelu(x, approximate=True)

def _silu(x):
    return jax.nn.silu(x)

def _sigmoid(x):
    return jax.nn.sigmoid(x)

def _layernorm(x, axis=-1, eps=1e-05):
    m = jnp.mean(x, axis=axis, keepdims=True)
    v = jnp.var(x, axis=axis, keepdims=True)
    return (x - m) / jnp.sqrt(v + eps)

def _scatter_add(tgt, idx, src, axis=0):
    return tgt.at[idx].add(src)

def _segment_sum(src, seg, n):
    return jax.ops.segment_sum(src, seg, n)
kernel_name = 'mk_adj_resnorm_d1_adj_r2_f619af'

def setup_inputs(seed: int=0):
    np.random.seed(seed)
    _w = jnp.asarray

    def _rec_inputs():
        import jax
        import jax.numpy as jnp
        _gk = jax.random.key(seed)
        x = -0.0002928 + 1 * jax.random.normal(jax.random.fold_in(_gk, 1), (8, 1024, 128), jnp.float32)
        _w = (1.0 + jnp.arange(1024, dtype=jnp.float32)) ** (-0.5)
        _w = _w / _w.mean()
        _pij = jnp.clip(0.015625 * _w[:, None] * _w[None, :], 0.0, 1.0)
        _a = jax.random.uniform(jax.random.fold_in(_gk, 2), (8, 1024, 1024)) < _pij
        adj = _a.astype(jnp.int32)
        return (x, adj)
    x, adj = _rec_inputs()

    def _L0_gnn_setup():
        import jax, jax.numpy as jnp
        import numpy as np
        B, N, D_IN, D_OUT, R = (8, 1024, 128, 128, 4)
        key = jax.random.key(seed)
        k1, k2, k3, k4 = jax.random.split(key, 4)
        x = jax.random.normal(k1, (B, N, D_IN), dtype=jnp.float32)
        adj = jnp.zeros((1,), dtype=jnp.float32)
        relation = jax.random.randint(k2, (B, N, N), 0, R + 1, dtype=jnp.int32)
        weight = jax.random.normal(k3, (R, D_IN, D_OUT), dtype=jnp.float32) * 0.05
        bias = jax.random.normal(k4, (D_OUT,), dtype=jnp.float32) * 0.05
        return {'x': x, 'adj': adj, 'relation': relation, 'weight': weight, 'bias': bias}
    _L0_gnn_all = _L0_gnn_setup()
    _L0_gnn_in = {k: v for k, v in _L0_gnn_all.items() if k in ('adj', 'weight', 'bias')}
    del _L0_gnn_all
    return {'x': x, 'adj': adj, 'L0_gnn_adj': _L0_gnn_in['adj'], 'L0_gnn_weight': _L0_gnn_in['weight'], 'L0_gnn_bias': _L0_gnn_in['bias']}

def reference(x, adj, L0_gnn_adj, L0_gnn_weight, L0_gnn_bias):
    import jax
    import jax.numpy as jnp

    def _L0_gnn_ref(x, adj, relation, weight, bias):
        import jax, jax.numpy as jnp
        import numpy as np
        B, N, D_IN, D_OUT, R = (8, 1024, 128, 128, 4)
        rel_ids = jnp.arange(1, weight.shape[0] + 1, dtype=relation.dtype)
        masks = (relation[None] == rel_ids[:, None, None, None]).astype(x.dtype)
        h = jnp.einsum('rbnm,bmd->rbnd', masks, x)
        y = jnp.einsum('rbnd,rdo->bno', h, weight)
        return y + bias
    x = _layernorm(x + _L0_gnn_ref(x, L0_gnn_adj, adj, L0_gnn_weight, L0_gnn_bias), axis=-1)
    return x

_drawn_inputs = setup_inputs


def setup_inputs(seed=0):
    import zlib

    import numpy as np

    out = dict(_drawn_inputs(seed))
    spreads = {}
    factors = {}
    for name, (base, spread) in spreads.items():
        noise = np.random.default_rng([zlib.crc32(name.encode()), seed]).standard_normal(out[name].shape)
        drawn = base * np.exp(spread * noise) if base else spread * noise
        out[name] = jnp.asarray(drawn.astype(out[name].dtype))
    for name, factor in factors.items():
        out[name] = (out[name] * factor).astype(out[name].dtype)
    return out
```

```python
import concourse.bass as bass
from concourse import mybir
from contextlib import ExitStack


Q = 4
LANES = 32
WORD = 2
HALVES = 2
PARTS = 3
SHARP = 20.0


def relational_layer(nc, x, adj, weight, bias, out):
    fp32, bf16, fp16 = mybir.dt.float32, mybir.dt.bfloat16, mybir.dt.float16
    i32, u32 = mybir.dt.int32, mybir.dt.uint32
    ALU, ACT, AX = mybir.AluOpType, mybir.ActivationFunctionType, mybir.AxisListType

    B, N, D = x.shape
    R = weight.shape[0]
    P = Q * LANES
    MQ = N // Q
    J = MQ // (WORD * LANES)
    TILES = J * WORD
    ROWS = N // HALVES
    G = ROWS // LANES
    PIECES = 2
    GP = G // PIECES
    NADJ = 4
    EPS = 1e-5
    CHUNKS = HALVES * B

    x_q = x.rearrange("b (q j k e) d -> b q k j (e d)", q=Q, j=J, k=LANES, e=WORD)
    out_q = out.rearrange("b (q j k e) d -> b q k j (e d)", q=Q, j=J, k=LANES, e=WORD)
    adj_q = adj.rearrange("b (h t k e) (q m) -> b h q e k t m", h=HALVES, k=LANES, e=WORD, q=Q)

    ctx = ExitStack()
    with ctx:
        def sb(name, shape, dt):
            return ctx.enter_context(nc.sbuf_tensor(name, shape, dt))

        def pb(name, shape, dt):
            return ctx.enter_context(nc.psum_tensor(name, shape, dt))

        def sem(name):
            return ctx.enter_context(nc.semaphore(name))

        adj_sb = sb("adj_sb", [P, NADJ, G, MQ], i32)
        mask = sb("mask", [P, 2, G, MQ], fp16)
        maskT = sb("maskT", [P, 2, G, J, LANES, WORD], fp16)
        x_sb = sb("x_sb", [P, 2, J, WORD * D], fp32)
        x_rest = sb("x_rest", [P, TILES * D], fp32)
        x_part = sb("x_part", [P, 2, PARTS, TILES, D], bf16)
        x_bias = sb("x_bias", [P, 2, TILES, D], fp32)
        h_sb = sb("h_sb", [P, 2, TILES, P], fp32)
        h_all = sb("h_all", [P, R, TILES, P], fp32)
        w_sb = sb("w_sb", [P, R, D], fp32)
        bias_sb = sb("bias_sb", [P, D], fp32)
        s_sb = sb("s_sb", [P, 2, TILES, D], fp32)
        stats = sb("stats", [P, 2, TILES, 6], fp32)
        small = sb("small", [P, 8, TILES], fp32)
        power = sb("power", [P, TILES], fp32)
        quarter = sb("quarter", [P, TILES], fp32)
        scale = sb("scale", [P, 2, TILES], fp32)
        shift = sb("shift", [P, 2, TILES], fp32)
        out_sb = sb("out_sb", [P, 2, TILES, D], fp32)
        sums = sb("sums", [P, 2, HALVES * PIECES], fp32)
        most = sb("most", [P, HALVES * PIECES], fp32)
        most_1 = sb("most_1", [P, 1], fp32)
        above = sb("above", [P, 1], fp32)
        scratch = sb("scratch", [P, 1], fp32)
        ones = sb("ones", [P, 1], fp32)
        flag = sb("flag", [1, 1], i32)
        minus_sharp = sb("minus_sharp", [P, 1], fp32)

        h_ps = pb("h_ps", [P, 2 * HALVES, ROWS], fp32)
        y_ps = pb("y_ps", [P, 2, TILES, D], fp32)

        const_loaded = sem("const_loaded")
        const_set = sem("const_set")
        x_loaded = [sem(f"x_loaded{s}") for s in range(2)]
        adj_loaded = [sem(f"adj_loaded{s}") for s in range(NADJ)]
        masked = sem("masked")
        tallied = sem("tallied")
        transposed = sem("transposed")
        x_split = sem("x_split")
        split_step = sem("split_step")
        biased = sem("biased")
        multiplied = sem("multiplied")
        h_copied = sem("h_copied")
        projected = sem("projected")
        added = sem("added")
        statistics = sem("statistics")
        scaled = sem("scaled")
        scale_step = sem("scale_step")
        normed = sem("normed")
        stored = [sem(f"stored{s}") for s in range(2)]
        flag_step = sem("flag_step")
        flag_counted = sem("flag_counted")
        flag_ready = sem("flag_ready")
        g_loaded = sem("g_loaded")
        g_split = sem("g_split")
        g_split_step = sem("g_split_step")
        g_masked = sem("g_masked")
        g_transposed = sem("g_transposed")
        g_multiplied = sem("g_multiplied")
        g_h_copied = sem("g_h_copied")
        g_projected = sem("g_projected")
        g_added = sem("g_added")
        g_statistics = sem("g_statistics")
        g_scaled = sem("g_scaled")
        g_scale_step = sem("g_scale_step")
        g_normed = sem("g_normed")
        g_stored = sem("g_stored")

        def load_adj(eng, b, hf, slot, quadrants, done):
            for q in quadrants:
                for e in range(WORD):
                    eng.dma_start(adj_sb[q * LANES:(q + 1) * LANES, slot].rearrange("p (t e) m -> p e t m", e=WORD)[:, e],
                                  adj_q[b, hf, q, e]).then_inc(done, 16)

        def load_x(eng, b, slot, done):
            for q in range(Q):
                eng.dma_start(x_sb[q * LANES:(q + 1) * LANES, slot], x_q[b, q]).then_inc(done, 16)

        def store(eng, b, slot, done):
            for q in range(Q):
                eng.dma_start(out_q[b, q], out_sb[q * LANES:(q + 1) * LANES, slot]
                              .rearrange("p (j e) d -> p j (e d)", j=J)).then_inc(done, 16)

        def split_x(pool, slot, step, step_base, split_done, bias_done):
            xs = x_sb[:, slot].rearrange("p j (e d) -> p (j e d)", e=WORD)
            xt = x_sb[:, slot].rearrange("p j (e d) -> p (j e) d", e=WORD)
            part = [x_part[:, slot, n].rearrange("p t d -> p (t d)") for n in range(PARTS)]
            nc.gpsimd.tensor_tensor(scratch[:, :], ones[:, :], ones[:, :], ALU.mult)
            nc.gpsimd.tensor_copy(part[0], xs).then_inc(step, 1)
            pool.wait_ge(step, step_base + 1)
            nc.gpsimd.tensor_tensor(x_rest[:, :], xs, part[0], ALU.subtract).then_inc(step, 1)
            pool.wait_ge(step, step_base + 2)
            nc.gpsimd.tensor_tensor(scratch[:, :], ones[:, :], ones[:, :], ALU.mult)
            nc.gpsimd.tensor_copy(part[1], x_rest[:, :]).then_inc(step, 1)
            pool.wait_ge(step, step_base + 3)
            nc.gpsimd.tensor_tensor(part[2], x_rest[:, :], part[1], ALU.subtract).then_inc(split_done, 1)
            nc.gpsimd.tensor_tensor(x_bias[:, slot], xt, bias_sb[:, :].unsqueeze(1).to_broadcast([P, TILES, D]),
                                    ALU.add).then_inc(bias_done, 1)

        def row_scales(pool, slot, step, base, done):
            st = stats[:, slot]
            even, odd, m2_even, m2_odd = st[:, :, 1], st[:, :, 4], st[:, :, 2], st[:, :, 5]
            a = [small[:, n] for n in range(8)]
            nc.gpsimd.tensor_tensor(a[0], even, odd, ALU.add)
            nc.gpsimd.tensor_tensor(a[1], even, odd, ALU.subtract)
            nc.gpsimd.tensor_tensor(a[2], m2_even, m2_odd, ALU.add).then_inc(step, 1)
            pool.wait_ge(step, base + 1)
            nc.gpsimd.tensor_tensor(a[3], a[1], a[1], ALU.mult)
            nc.gpsimd.tensor_scalar(a[4], a[2], 1.0 / D, EPS, ALU.mult, ALU.add).then_inc(step, 1)
            pool.wait_ge(step, base + 2)
            nc.gpsimd.tensor_tensor(a[5], a[3], quarter[:, :], ALU.mult).then_inc(step, 1)
            pool.wait_ge(step, base + 3)
            nc.gpsimd.tensor_tensor(a[6], a[4], a[5], ALU.add).then_inc(step, 1)
            pool.wait_ge(step, base + 4)
            nc.gpsimd.tensor_tensor(scale[:, slot], a[6], power[:, :], ALU.pow)
            nc.gpsimd.tensor_scalar(a[7], a[0], -0.5, 0.0, ALU.mult, ALU.add).then_inc(step, 1)
            pool.wait_ge(step, base + 5)
            nc.gpsimd.tensor_tensor(shift[:, slot], a[7], scale[:, slot], ALU.mult).then_inc(done, 1)

        def add_and_measure(dve, slot, add_done, add_count, stat_done):
            nc.vector.tensor_tensor(s_sb[:, slot], y_ps[:, slot], x_bias[:, slot], ALU.add).then_inc(add_done, 1)
            dve.wait_ge(add_done, add_count)
            for t in range(TILES):
                last = nc.vector.bn_stats(stats[:, slot, t, :], s_sb[:, slot, t, :])
            last.then_inc(stat_done, 1)

        def normalize(slot, done):
            for t in range(TILES):
                last = nc.vector.tensor_scalar(out_sb[:, slot, t, :], s_sb[:, slot, t, :], scale[:, slot, t:t + 1],
                                               shift[:, slot, t:t + 1], ALU.mult, ALU.add)
            last.then_inc(done, 1)

        def transpose_blocks(src, dst):
            return nc.vector.transpose(dst.rearrange("p g j i e -> p (g j i e)").bitcast(u32),
                                       src.rearrange("p g m -> p (g m)").bitcast(u32))

        def neighbour_products(hf, bank, slot):
            for j in range(J):
                for e in range(WORD):
                    for part in range(PARTS):
                        step = (j * WORD + e) * PARTS + part
                        last = nc.tensor.matmul(h_ps[:, bank], x_part[:, slot, part, j * WORD + e, :],
                                                maskT[:, hf, :, j, :, e],
                                                start=(step == 0), stop=(step == TILES * PARTS - 1))
            return last

        def by_tile(h, hf):
            quarters = slice(hf * Q // HALVES * LANES, (hf + 1) * Q // HALVES * LANES)
            return h[:, :, quarters].rearrange("p t (q k) -> p q t k", k=LANES)

        def by_half(h):
            return h.rearrange("p (q t k) -> p q t k", q=Q // HALVES, k=LANES)

        def project(h_of, slot, relations):
            for j in range(J):
                for e in range(WORD):
                    for r in range(relations):
                        last = nc.tensor.matmul(y_ps[:, slot, j * WORD + e, :], h_of(r)[:, j * WORD + e], w_sb[:, r, :],
                                                start=(r == 0), stop=(r == relations - 1))
            return last

        def over_batches(eng, step):
            def pair(u):
                for slot in range(2):
                    step(u, slot)
            pair(0)
            with eng.Fori(1, B // 2 - 1) as u:
                pair(u)
            pair(B // 2 - 1)

        def reached(n, least):
            return n >= least if type(n) is int else True

        def within(n, end):
            return n < end if type(n) is int else True

        def load_ahead(eng, u, slot, hf, quadrants):
            b = 2 * u + slot
            c = HALVES * b + hf
            if not within(c + 3, CHUNKS):
                return
            if reached(c, 1):
                eng.wait_ge(masked, PIECES * c)
            load_adj(eng, b + 1 + hf, 1 - hf, (HALVES * slot + hf + 3) % NADJ, quadrants,
                     adj_loaded[(HALVES * slot + hf + 3) % NADJ])

        block = ctx.enter_context(nc.Block())

        @block.sync
        def _(sp):
            load_x(sp, 0, 0, x_loaded[0])
            for c in range(3):
                load_adj(sp, c // HALVES, c % HALVES, c, (0, 1), adj_loaded[c])
                if c == 0:
                    sp.dma_start(w_sb[:, :, :], weight.rearrange("r d o -> d r o")).then_inc(const_loaded, 16)
                    sp.dma_start(bias_sb[:, :], bias.unsqueeze(0).to_broadcast([P, D])).then_inc(const_loaded, 16)
                    load_x(sp, 1, 1, x_loaded[1])

            def step(u, slot):
                b = 2 * u + slot
                for hf in range(HALVES):
                    load_ahead(sp, u, slot, hf, (0, 1))
                if within(b + 2, B):
                    sp.wait_ge(x_split, b + 1)
                    sp.wait_ge(biased, b + 1)
                    load_x(sp, b + 2, slot, x_loaded[slot])
                if reached(b, 2):
                    sp.wait_ge(normed, b - 1)
                    store(sp, b - 2, slot, stored[slot])

            over_batches(sp, step)
            for b in (B - 2, B - 1):
                sp.wait_ge(normed, b + 1)
                store(sp, b, b % 2, stored[b % 2])
            for slot in range(2):
                sp.wait_ge(stored[slot], 16 * Q * B // 2)
            sp.wait_ge(flag_ready, 1)
            again = sp.value_load(flag[0:1, 0:1], min_val=0, max_val=P)
            with sp.If(again > 0):
                sp.sem_inc(g_stored, 16 * Q)
                with sp.Fori(0, B) as b:
                    sp.wait_ge(g_stored, 16 * Q * (b + 1))
                    load_x(sp, b, 0, g_loaded)
                    for hf in range(HALVES):
                        load_adj(sp, b, hf, hf, range(Q), g_loaded)
                    sp.wait_ge(g_normed, b + 1)
                    store(sp, b, 0, g_stored)
                sp.wait_ge(g_stored, 16 * Q * (B + 1))
            sp.end_ifs()

        @block.gpsimd
        def _(pool):
            nc.gpsimd.memset(power[:, :], -0.5)
            nc.gpsimd.memset(quarter[:, :], 0.25)
            nc.gpsimd.memset(ones[:, :], 1.0)
            nc.gpsimd.memset(minus_sharp[:, :], -SHARP).then_inc(const_set, 1)
            pool.wait_ge(const_set, 1)
            pool.wait_ge(const_loaded, 32)

            def split(u, slot):
                b = 2 * u + slot
                pool.wait_ge(x_loaded[slot], 16 * Q * (u + 1))
                if reached(b, 2):
                    pool.wait_ge(multiplied, HALVES * (b - 1))
                    pool.wait_ge(added, b - 1)
                split_x(pool, slot, split_step, 3 * b, x_split, biased)

            def scales(b, slot):
                pool.wait_ge(statistics, b + 1)
                if reached(b, 2):
                    pool.wait_ge(normed, b - 1)
                row_scales(pool, slot, scale_step, 5 * b, scaled)

            def step(u, slot):
                b = 2 * u + slot
                if within(b + 1, B):
                    split(u + slot, 1 - slot)
                if reached(b, 1):
                    scales(b - 1, 1 - slot)

            split(0, 0)
            over_batches(pool, step)
            scales(B - 1, 1)

            pool.wait_ge(flag_ready, 1)
            again = pool.value_load(flag[0:1, 0:1], min_val=0, max_val=P)
            with pool.If(again > 0):
                with pool.Fori(0, B) as b:
                    pool.wait_ge(g_loaded, 16 * Q * (1 + WORD * HALVES) * (b + 1))
                    split_x(pool, 0, g_split_step, 3 * b, g_split, g_split)
                    pool.wait_ge(g_statistics, b + 1)
                    row_scales(pool, 0, g_scale_step, 5 * b, g_scaled)
            pool.end_ifs()

        @block.scalar
        def _(act):
            for c in range(3):
                load_adj(act, c // HALVES, c % HALVES, c, (2, 3), adj_loaded[c])
            act.wait_ge(const_set, 1)

            def copy_h(b, slot, hf):
                act.wait_ge(multiplied, HALVES * b + hf + 1)
                if reached(b, 2):
                    act.wait_ge(projected, b - 1)
                nc.scalar.copy(by_tile(h_sb[:, slot], hf), by_half(h_ps[:, HALVES * slot + hf])).then_inc(h_copied, 1)

            def step(u, slot):
                b = 2 * u + slot
                for hf in range(HALVES):
                    c = HALVES * b + hf
                    load_ahead(act, u, slot, hf, (2, 3))
                    s = HALVES * slot + hf
                    act.wait_ge(adj_loaded[s], 16 * Q * WORD * (u + 1))
                    if reached(c, 2):
                        act.wait_ge(transposed, PIECES * (c - 1))
                    if reached(b, 2):
                        act.wait_ge(tallied, b - 1)
                    for pc in range(PIECES):
                        g = slice(pc * GP, (pc + 1) * GP)
                        nc.scalar.activation(mask[:, hf, g].rearrange("p g m -> p (g m)"),
                                             adj_sb[:, s, g].rearrange("p g m -> p (g m)"), ACT.Exp,
                                             scale=SHARP, bias=minus_sharp[:, 0:1],
                                             accum_out=sums[:, slot, hf * PIECES + pc:hf * PIECES + pc + 1]
                                             ).then_inc(masked, 1)
                    if hf == 1:
                        copy_h(b, slot, 0)
                    elif reached(b, 1):
                        copy_h(b - 1, 1 - slot, 1)

            over_batches(act, step)
            copy_h(B - 1, 1, 1)

            act.wait_ge(flag_ready, 1)
            again = act.value_load(flag[0:1, 0:1], min_val=0, max_val=P)
            with act.If(again > 0):
                with act.Fori(0, B) as b:
                    with act.Fori(0, R) as r:
                        for hf in range(HALVES):
                            act.wait_ge(g_multiplied, HALVES * R * b + HALVES * r + hf + 1)
                            nc.scalar.copy(by_tile(h_all[:, r], hf), by_half(h_ps[:, hf])).then_inc(g_h_copied, 1)
            act.end_ifs()

        @block.vector
        def _(dve):
            nc.vector.memset(most[:, :], 0.0).then_inc(flag_step, 1)
            dve.wait_ge(flag_step, 1)

            def measure(b, slot):
                dve.wait_ge(projected, b + 1)
                dve.wait_ge(biased, b + 1)
                if reached(b, 2):
                    dve.wait_ge(normed, b - 1)
                    dve.wait_ge(scaled, b - 1)
                add_and_measure(dve, slot, added, b + 1, statistics)

            def finish(b, slot, u):
                dve.wait_ge(scaled, b + 1)
                if reached(u, 1):
                    dve.wait_ge(stored[slot], 16 * Q * u)
                normalize(slot, normed)

            def step(u, slot):
                b = 2 * u + slot
                for hf in range(HALVES):
                    c = HALVES * b + hf
                    if reached(c, 2):
                        dve.wait_ge(multiplied, c - 1)
                    for pc in range(PIECES):
                        dve.wait_ge(masked, PIECES * c + pc + 1)
                        g = slice(pc * GP, (pc + 1) * GP)
                        transpose_blocks(mask[:, hf, g], maskT[:, hf, g]).then_inc(transposed, 1)
                    if hf == 0 and reached(b, 2):
                        finish(b - 2, slot, u - 1)
                if reached(b, 1):
                    measure(b - 1, 1 - slot)
                    dve.wait_ge(tallied, b)
                nc.vector.tensor_tensor(most[:, :], most[:, :], sums[:, slot], ALU.max).then_inc(tallied, 1)

            over_batches(dve, step)
            dve.wait_ge(tallied, B)
            nc.vector.reduce_max(most_1[:, :], most[:, :], AX.X).then_inc(flag_step, 1)
            dve.wait_ge(flag_step, 2)
            nc.vector.tensor_scalar(above[:, :], most_1[:, :], GP * MQ + 0.5, None, ALU.is_gt).then_inc(flag_step, 1)
            finish(B - 2, 0, B // 2 - 1)
            measure(B - 1, 1)
            dve.wait_ge(flag_counted, 1)
            nc.vector.tensor_copy(flag[:, :], h_ps[0:1, 0, 0:1]).then_inc(flag_ready, 1)
            finish(B - 1, 1, B // 2 - 1)

            dve.wait_ge(flag_ready, 1)
            again = dve.value_load(flag[0:1, 0:1], min_val=0, max_val=P)
            with dve.If(again > 0):
                with dve.Fori(0, B) as b:
                    dve.wait_ge(g_loaded, 16 * Q * (1 + WORD * HALVES) * (b + 1))
                    for r in range(R):
                        for hf in range(HALVES):
                            k = HALVES * r + hf
                            if k >= 2:
                                dve.wait_ge(g_transposed, HALVES * R * b + k - 1)
                            nc.vector.tensor_scalar(mask[:, hf].rearrange("p g m -> p (g m)"),
                                                    adj_sb[:, hf].rearrange("p g m -> p (g m)"),
                                                    float(r + 1), None, ALU.is_equal).then_inc(g_masked, 1)
                            dve.wait_ge(g_masked, HALVES * R * b + k + 1)
                            if k >= 2:
                                dve.wait_ge(g_multiplied, HALVES * R * b + k - 1)
                            transpose_blocks(mask[:, hf], maskT[:, hf]).then_inc(g_transposed, 1)
                    dve.wait_ge(g_projected, b + 1)
                    dve.wait_ge(g_split, 2 * (b + 1))
                    add_and_measure(dve, 0, g_added, b + 1, g_statistics)
                    dve.wait_ge(g_scaled, b + 1)
                    normalize(0, g_normed)
            dve.end_ifs()

        @block.tensor
        def _(pe):
            def step(u, slot):
                b = 2 * u + slot
                for hf in range(HALVES):
                    c = HALVES * b + hf
                    pe.wait_ge(x_split, b + 1)
                    pe.wait_ge(transposed, PIECES * (c + 1))
                    if reached(c, 4):
                        pe.wait_ge(h_copied, c - 3)
                    neighbour_products(hf, HALVES * slot + hf, slot).then_inc(multiplied, 1)
                    if hf == 0 and reached(b, 1):
                        finish(b - 1, 1 - slot)

            def finish(b, slot):
                pe.wait_ge(h_copied, HALVES * (b + 1))
                if reached(b, 2):
                    pe.wait_ge(added, b - 1)
                project(lambda r: h_sb[:, slot], slot, 1).then_inc(projected, 1)

            pe.wait_ge(const_loaded, 32)
            over_batches(pe, step)
            finish(B - 1, 1)
            pe.wait_ge(flag_step, 3)
            pe.wait_ge(h_copied, CHUNKS)
            nc.tensor.matmul(h_ps[0:1, 0, 0:1], above[:, 0:1], ones[:, 0:1], start=True, stop=True).then_inc(flag_counted, 1)

            pe.wait_ge(flag_ready, 1)
            again = pe.value_load(flag[0:1, 0:1], min_val=0, max_val=P)
            with pe.If(again > 0):
                with pe.Fori(0, B) as b:
                    with pe.Fori(0, R) as r:
                        for hf in range(HALVES):
                            pe.wait_ge(g_split, 2 * (b + 1))
                            pe.wait_ge(g_transposed, HALVES * R * b + HALVES * r + hf + 1)
                            neighbour_products(hf, hf, 0).then_inc(g_multiplied, 1)
                            pe.wait_ge(g_h_copied, HALVES * R * b + HALVES * r + hf + 1)
                            pe.wait_ge(flag_ready, 1)
                    project(lambda r: h_all[:, r], 0, R).then_inc(g_projected, 1)
            pe.end_ifs()


_INS = ['x', 'adj', 'L0_gnn_weight', 'L0_gnn_bias']


def kernel(**inputs):
    import numpy as _np
    import concourse.bacc as _bacc
    from concourse import mybir as _mybir
    from concourse.bass_utils import run_bass_kernel_spmd as _run

    nc = _bacc.Bacc("TRN2", target_bir_lowering=False, num_devices=1)
    arrays, args = {}, []
    for name in _INS:
        a = _np.ascontiguousarray(inputs[name])
        arrays[f"in_{name}_dram"] = a
        args.append(nc.dram_tensor(f"in_{name}_dram", a.shape, _mybir.dt.from_np(a.dtype), kind="ExternalInput").ap())
    x = inputs['x']
    out = nc.dram_tensor("out_0_dram", x.shape, _mybir.dt.from_np(_np.dtype(x.dtype)), kind="ExternalOutput").ap()
    relational_layer(nc, *args, out)
    r = _run(nc, [arrays], core_ids=[0])
    return r.results[0]["out_0_dram"]
```

```python
import concourse.bass as bass
from concourse import mybir
from contextlib import ExitStack


Q = 4
LANES = 32
WORD = 4
HALVES = 2
PARTS = 3
ONE_BITS = 0x38
OTHER_BITS = 0xFFFFFFFF ^ (ONE_BITS * 0x01010101)


def relational_layer(nc, x, adj, weight, bias, out):
    fp32, bf16, fp8 = mybir.dt.float32, mybir.dt.bfloat16, mybir.dt.float8e4
    i32, u32 = mybir.dt.int32, mybir.dt.uint32
    ALU, ACT, AX = mybir.AluOpType, mybir.ActivationFunctionType, mybir.AxisListType

    B, N, D = x.shape
    R = weight.shape[0]
    P = Q * LANES
    MQ = N // Q
    J = MQ // (WORD * LANES)
    TILES = J * WORD
    ROWS = N // HALVES
    G = ROWS // LANES
    PIECES = 2
    GP = G // PIECES
    NADJ = 4
    EPS = 1e-5
    CHUNKS = HALVES * B

    x_p = x.rearrange("b (p t) d -> b p (t d)", p=P)
    out_p = out.rearrange("b (p t) d -> b p (t d)", p=P)
    adj_q = adj.rearrange("b (h g i) (q m) -> b h q i g m", h=HALVES, i=LANES, q=Q)

    ctx = ExitStack()
    with ctx:
        def sb(name, shape, dt):
            return ctx.enter_context(nc.sbuf_tensor(name, shape, dt))

        def pb(name, shape, dt):
            return ctx.enter_context(nc.psum_tensor(name, shape, dt))

        def sem(name):
            return ctx.enter_context(nc.semaphore(name))

        adj_sb = sb("adj_sb", [P, NADJ, G, MQ], i32)
        mask = sb("mask", [P, 2, G, MQ], fp8)
        maskT = sb("maskT", [P, 2, G, J, LANES, WORD], fp8)
        x_sb = sb("x_sb", [P, 2, TILES, D], fp32)
        x_rest = sb("x_rest", [P, TILES * D], fp32)
        x_part = sb("x_part", [P, 2, PARTS, TILES, D], bf16)
        x_bias = sb("x_bias", [P, 2, TILES, D], fp32)
        h_sb = sb("h_sb", [P, 2, TILES, P], fp32)
        h_all = sb("h_all", [P, R, TILES, P], fp32)
        w_sb = sb("w_sb", [P, R, D], fp32)
        bias_sb = sb("bias_sb", [P, D], fp32)
        s_sb = sb("s_sb", [P, 2, TILES, D], fp32)
        stats = sb("stats", [P, 2, TILES, 6], fp32)
        small = sb("small", [P, 8, TILES], fp32)
        power = sb("power", [P, TILES], fp32)
        quarter = sb("quarter", [P, TILES], fp32)
        scale = sb("scale", [P, 2, TILES], fp32)
        shift = sb("shift", [P, 2, TILES], fp32)
        out_sb = sb("out_sb", [P, 2, TILES, D], fp32)
        seen = sb("seen", [P, GP * MQ // WORD], u32)
        above = sb("above", [P, 2], fp32)
        scratch = sb("scratch", [P, 1], fp32)
        ones = sb("ones", [P, 1], fp32)
        flag = sb("flag", [1, 1], i32)

        h_ps = pb("h_ps", [P, 2 * HALVES, ROWS], fp32)
        y_ps = pb("y_ps", [P, 2, TILES, D], fp32)

        const_loaded = sem("const_loaded")
        const_set = sem("const_set")
        x_loaded = [sem(f"x_loaded{s}") for s in range(2)]
        adj_loaded = [sem(f"adj_loaded{s}") for s in range(NADJ)]
        masked = sem("masked")
        collected = sem("collected")
        coarse = sem("coarse")
        rest_made = sem("rest_made")
        middle = sem("middle")
        transposed = sem("transposed")
        x_split = sem("x_split")
        biased = sem("biased")
        multiplied = sem("multiplied")
        h_copied = sem("h_copied")
        projected = sem("projected")
        added = sem("added")
        statistics = sem("statistics")
        scaled = sem("scaled")
        scale_step = sem("scale_step")
        normed = sem("normed")
        stored = [sem(f"stored{s}") for s in range(2)]
        flag_step = sem("flag_step")
        flag_counted = sem("flag_counted")
        flag_ready = sem("flag_ready")
        g_loaded = sem("g_loaded")
        g_split = sem("g_split")
        g_coarse = sem("g_coarse")
        g_rest_made = sem("g_rest_made")
        g_middle = sem("g_middle")
        g_masked = sem("g_masked")
        g_transposed = sem("g_transposed")
        g_multiplied = sem("g_multiplied")
        g_h_copied = sem("g_h_copied")
        g_projected = sem("g_projected")
        g_added = sem("g_added")
        g_statistics = sem("g_statistics")
        g_scaled = sem("g_scaled")
        g_scale_step = sem("g_scale_step")
        g_normed = sem("g_normed")
        g_stored = sem("g_stored")

        def load_adj(eng, b, hf, slot, quadrants, done):
            for q in quadrants:
                eng.dma_start(adj_sb[q * LANES:(q + 1) * LANES, slot], adj_q[b, hf, q]).then_inc(done, 16)

        def load_x(eng, b, slot, done):
            eng.dma_start(flat(x_sb[:, slot]), x_p[b]).then_inc(done, 16)

        def store(eng, b, slot, done):
            eng.dma_start(out_p[b], flat(out_sb[:, slot])).then_inc(done, 16)

        def flat(tiles):
            return tiles.rearrange("p t d -> p (t d)")

        def round_coarse(slot, done):
            nc.vector.tensor_copy(flat(x_part[:, slot, 0]), flat(x_sb[:, slot])).then_inc(done, 1)

        def take_rest(slot, done):
            nc.gpsimd.tensor_tensor(x_rest[:, :], flat(x_sb[:, slot]), flat(x_part[:, slot, 0]),
                                    ALU.subtract).then_inc(done, 1)

        def round_middle(slot, done):
            nc.vector.tensor_copy(flat(x_part[:, slot, 1]), x_rest[:, :]).then_inc(done, 1)

        def take_fine(slot, done):
            nc.gpsimd.tensor_tensor(flat(x_part[:, slot, 2]), x_rest[:, :], flat(x_part[:, slot, 1]),
                                    ALU.subtract).then_inc(done, 1)

        def add_bias(slot, done):
            nc.gpsimd.tensor_tensor(x_bias[:, slot], x_sb[:, slot],
                                    bias_sb[:, :].unsqueeze(1).to_broadcast([P, TILES, D]), ALU.add).then_inc(done, 1)

        def row_scales(pool, slot, step, base, done):
            st = stats[:, slot]
            even, odd, m2_even, m2_odd = st[:, :, 1], st[:, :, 4], st[:, :, 2], st[:, :, 5]
            a = [small[:, n] for n in range(8)]
            nc.gpsimd.tensor_tensor(a[0], even, odd, ALU.add)
            nc.gpsimd.tensor_tensor(a[1], even, odd, ALU.subtract)
            nc.gpsimd.tensor_tensor(a[2], m2_even, m2_odd, ALU.add).then_inc(step, 1)
            pool.wait_ge(step, base + 1)
            nc.gpsimd.tensor_tensor(a[3], a[1], a[1], ALU.mult)
            nc.gpsimd.tensor_scalar(a[4], a[2], 1.0 / D, EPS, ALU.mult, ALU.add).then_inc(step, 1)
            pool.wait_ge(step, base + 2)
            nc.gpsimd.tensor_tensor(a[5], a[3], quarter[:, :], ALU.mult).then_inc(step, 1)
            pool.wait_ge(step, base + 3)
            nc.gpsimd.tensor_tensor(a[6], a[4], a[5], ALU.add).then_inc(step, 1)
            pool.wait_ge(step, base + 4)
            nc.gpsimd.tensor_tensor(scale[:, slot], a[6], power[:, :], ALU.pow)
            nc.gpsimd.tensor_scalar(a[7], a[0], -0.5, 0.0, ALU.mult, ALU.add).then_inc(step, 1)
            pool.wait_ge(step, base + 5)
            nc.gpsimd.tensor_tensor(shift[:, slot], a[7], scale[:, slot], ALU.mult).then_inc(done, 1)

        def add_and_measure(dve, slot, add_done, add_count, stat_done):
            nc.vector.tensor_tensor(s_sb[:, slot], y_ps[:, slot], x_bias[:, slot], ALU.add).then_inc(add_done, 1)
            dve.wait_ge(add_done, add_count)
            for t in range(TILES):
                last = nc.vector.bn_stats(stats[:, slot, t, :], s_sb[:, slot, t, :])
            last.then_inc(stat_done, 1)

        def normalize(slot, done):
            for t in range(TILES):
                last = nc.vector.tensor_scalar(out_sb[:, slot, t, :], s_sb[:, slot, t, :], scale[:, slot, t:t + 1],
                                               shift[:, slot, t:t + 1], ALU.mult, ALU.add)
            last.then_inc(done, 1)

        def words(values):
            return values.rearrange("p g m -> p (g m)").bitcast(u32)

        def transpose_blocks(src, dst):
            blocks = words(src).rearrange("p (g k j) -> p g j k", k=LANES, j=J)
            return nc.vector.transpose(dst.rearrange("p g j i e -> p (g j i e)").bitcast(u32), blocks)

        def neighbour_products(hf, bank, slot):
            nc.tensor.matmul(h_ps[:, bank, 0:1], x_part[:, slot, 0, 0, :], x_part[:, slot, 0, 0, 0:1],
                             start=True, stop=True)
            for t in range(TILES):
                for part in range(PARTS):
                    step = t * PARTS + part
                    last = nc.tensor.matmul(h_ps[:, bank], x_part[:, slot, part, t, :],
                                            maskT[:, hf, :, t // WORD, :, t % WORD],
                                            start=(step == 0), stop=(step == TILES * PARTS - 1))
            return last

        def copy_chunk(h, hf, bank):
            half = slice(hf * P // HALVES, (hf + 1) * P // HALVES)
            return nc.scalar.copy(h[:, :, half].rearrange("d t p -> d p t"),
                                  h_ps[:, bank].rearrange("d (p t) -> d p t", t=TILES))

        def project(h_of, slot, relations):
            for t in range(TILES):
                for r in range(relations):
                    last = nc.tensor.matmul(y_ps[:, slot, t, :], h_of(r)[:, t], w_sb[:, r, :],
                                            start=(r == 0), stop=(r == relations - 1))
            return last

        def over_batches(eng, step):
            def pair(u):
                for slot in range(2):
                    step(u, slot)
            pair(0)
            with eng.Fori(1, B // 2 - 1) as u:
                pair(u)
            pair(B // 2 - 1)

        def reached(n, least):
            return n >= least if type(n) is int else True

        def within(n, end):
            return n < end if type(n) is int else True

        def load_ahead(eng, u, slot, hf, quadrants):
            b = 2 * u + slot
            c = HALVES * b + hf
            if not within(c + 3, CHUNKS):
                return
            if reached(c, 1):
                eng.wait_ge(masked, PIECES * c)
            load_adj(eng, b + 1 + hf, 1 - hf, (HALVES * slot + hf + 3) % NADJ, quadrants,
                     adj_loaded[(HALVES * slot + hf + 3) % NADJ])

        block = ctx.enter_context(nc.Block())

        @block.sync
        def _(sp):
            load_x(sp, 0, 0, x_loaded[0])
            for c in range(3):
                load_adj(sp, c // HALVES, c % HALVES, c, (0, 1), adj_loaded[c])
                if c == 0:
                    sp.dma_start(w_sb[:, :, :], weight.rearrange("r d o -> d r o")).then_inc(const_loaded, 16)
                    sp.dma_start(bias_sb[:, :], bias.unsqueeze(0).to_broadcast([P, D])).then_inc(const_loaded, 16)
                    load_x(sp, 1, 1, x_loaded[1])

            def step(u, slot):
                b = 2 * u + slot
                for hf in range(HALVES):
                    load_ahead(sp, u, slot, hf, (0, 1))
                if within(b + 2, B):
                    sp.wait_ge(rest_made, b + 1)
                    sp.wait_ge(biased, b + 1)
                    load_x(sp, b + 2, slot, x_loaded[slot])
                if reached(b, 2):
                    sp.wait_ge(normed, b - 1)
                    store(sp, b - 2, slot, stored[slot])

            over_batches(sp, step)
            for b in (B - 2, B - 1):
                sp.wait_ge(normed, b + 1)
                store(sp, b, b % 2, stored[b % 2])
            for slot in range(2):
                sp.wait_ge(stored[slot], 16 * B // 2)
            sp.wait_ge(flag_ready, 1)
            again = sp.value_load(flag[0:1, 0:1], min_val=0, max_val=P)
            with sp.If(again > 0):
                sp.sem_inc(g_stored, 16)
                with sp.Fori(0, B) as b:
                    sp.wait_ge(g_stored, 16 * (b + 1))
                    load_x(sp, b, 0, g_loaded)
                    for hf in range(HALVES):
                        load_adj(sp, b, hf, hf, range(Q), g_loaded)
                    sp.wait_ge(g_normed, b + 1)
                    store(sp, b, 0, g_stored)
                sp.wait_ge(g_stored, 16 * (B + 1))
            sp.end_ifs()

        @block.gpsimd
        def _(pool):
            nc.gpsimd.memset(power[:, :], -0.5)
            nc.gpsimd.memset(quarter[:, :], 0.25)
            nc.gpsimd.memset(ones[:, :], 1.0).then_inc(const_set, 1)
            pool.wait_ge(const_set, 1)
            pool.wait_ge(const_loaded, 32)

            def split(u, slot):
                b = 2 * u + slot
                pool.wait_ge(coarse, b + 1)
                if reached(b, 1):
                    pool.wait_ge(x_split, b)
                take_rest(slot, rest_made)
                if reached(b, 2):
                    pool.wait_ge(added, b - 1)
                add_bias(slot, biased)
                pool.wait_ge(middle, b + 1)
                take_fine(slot, x_split)

            def scales(b, slot):
                pool.wait_ge(statistics, b + 1)
                if reached(b, 2):
                    pool.wait_ge(normed, b - 1)
                row_scales(pool, slot, scale_step, 5 * b, scaled)

            def step(u, slot):
                b = 2 * u + slot
                if within(b + 1, B):
                    split(u + slot, 1 - slot)
                if reached(b, 1):
                    scales(b - 1, 1 - slot)

            split(0, 0)
            over_batches(pool, step)
            scales(B - 1, 1)

            pool.wait_ge(flag_ready, 1)
            again = pool.value_load(flag[0:1, 0:1], min_val=0, max_val=P)
            with pool.If(again > 0):
                with pool.Fori(0, B) as b:
                    pool.wait_ge(g_loaded, 16 * (1 + Q * HALVES) * (b + 1))
                    pool.wait_ge(g_coarse, b + 1)
                    take_rest(0, g_rest_made)
                    add_bias(0, g_split)
                    pool.wait_ge(g_middle, b + 1)
                    take_fine(0, g_split)
                    pool.wait_ge(g_statistics, b + 1)
                    row_scales(pool, 0, g_scale_step, 5 * b, g_scaled)
            pool.end_ifs()

        @block.scalar
        def _(act):
            for c in range(3):
                load_adj(act, c // HALVES, c % HALVES, c, (2, 3), adj_loaded[c])
            def copy_h(b, slot, hf):
                act.wait_ge(multiplied, HALVES * b + hf + 1)
                if reached(b, 2):
                    act.wait_ge(projected, b - 1)
                copy_chunk(h_sb[:, slot], hf, HALVES * slot + hf).then_inc(h_copied, 1)

            def step(u, slot):
                b = 2 * u + slot
                for hf in range(HALVES):
                    c = HALVES * b + hf
                    s = HALVES * slot + hf
                    act.wait_ge(adj_loaded[s], 16 * Q * (u + 1))
                    if reached(c, 2):
                        act.wait_ge(transposed, PIECES * (c - 1))
                        act.wait_ge(collected, PIECES * (c - 1) + 1)
                    load_ahead(act, u, slot, hf, (2, 3))
                    for pc in range(PIECES):
                        g = slice(pc * GP, (pc + 1) * GP)
                        nc.scalar.activation(mask[:, hf, g].rearrange("p g m -> p (g m)"),
                                             adj_sb[:, s, g].rearrange("p g m -> p (g m)"), ACT.Copy,
                                             saturate=False).then_inc(masked, 1)
                    if hf == 1:
                        copy_h(b, slot, 0)
                    elif reached(b, 1):
                        copy_h(b - 1, 1 - slot, 1)

            over_batches(act, step)
            copy_h(B - 1, 1, 1)

            act.wait_ge(flag_ready, 1)
            again = act.value_load(flag[0:1, 0:1], min_val=0, max_val=P)
            with act.If(again > 0):
                with act.Fori(0, B) as b:
                    with act.Fori(0, R) as r:
                        for hf in range(HALVES):
                            act.wait_ge(g_multiplied, HALVES * R * b + HALVES * r + hf + 1)
                            copy_chunk(h_all[:, r], hf, hf).then_inc(g_h_copied, 1)
            act.end_ifs()

        @block.vector
        def _(dve):
            nc.vector.memset(seen[:, :], 0).then_inc(collected, 1)

            def coarse_part(u, slot):
                b = 2 * u + slot
                dve.wait_ge(x_loaded[slot], 16 * (u + 1))
                if reached(b, 2):
                    dve.wait_ge(multiplied, HALVES * (b - 1))
                round_coarse(slot, coarse)

            def middle_part(b, slot):
                dve.wait_ge(rest_made, b + 1)
                round_middle(slot, middle)

            def measure(b, slot):
                dve.wait_ge(projected, b + 1)
                dve.wait_ge(biased, b + 1)
                if reached(b, 2):
                    dve.wait_ge(normed, b - 1)
                    dve.wait_ge(scaled, b - 1)
                add_and_measure(dve, slot, added, b + 1, statistics)

            def finish(b, slot, u):
                dve.wait_ge(scaled, b + 1)
                if reached(u, 1):
                    dve.wait_ge(stored[slot], 16 * u)
                normalize(slot, normed)

            def step(u, slot):
                b = 2 * u + slot
                for hf in range(HALVES):
                    c = HALVES * b + hf
                    if reached(c, 2):
                        dve.wait_ge(multiplied, c - 1)
                    for pc in range(PIECES):
                        dve.wait_ge(masked, PIECES * c + pc + 1)
                        g = slice(pc * GP, (pc + 1) * GP)
                        transpose_blocks(mask[:, hf, g], maskT[:, hf, g]).then_inc(transposed, 1)
                        dve.wait_ge(collected, PIECES * c + pc + 1)
                        nc.vector.tensor_tensor(seen[:, :], seen[:, :], words(mask[:, hf, g]),
                                                ALU.bitwise_or).then_inc(collected, 1)
                    if hf == 0 and within(b + 1, B):
                        coarse_part(u + slot, 1 - slot)
                    if hf == 0 and reached(b, 2):
                        finish(b - 2, slot, u - 1)
                if reached(b, 1):
                    measure(b - 1, 1 - slot)
                if within(b + 1, B):
                    middle_part(b + 1, 1 - slot)

            coarse_part(0, 0)
            middle_part(0, 0)
            over_batches(dve, step)
            dve.wait_ge(collected, PIECES * CHUNKS + 1)
            nc.vector.tensor_scalar(seen[:, :], seen[:, :], OTHER_BITS, None, ALU.bitwise_and).then_inc(flag_step, 1)
            dve.wait_ge(flag_step, 1)
            nc.vector.reduce_max(above[:, 0:1], seen[:, :], AX.X).then_inc(flag_step, 1)
            dve.wait_ge(flag_step, 2)
            nc.vector.tensor_scalar(above[:, 1:2], above[:, 0:1], 0.0, None, ALU.is_gt).then_inc(flag_step, 1)
            finish(B - 2, 0, B // 2 - 1)
            measure(B - 1, 1)
            dve.wait_ge(flag_counted, 1)
            nc.vector.tensor_copy(flag[:, :], h_ps[0:1, 0, 0:1]).then_inc(flag_ready, 1)
            finish(B - 1, 1, B // 2 - 1)

            dve.wait_ge(flag_ready, 1)
            again = dve.value_load(flag[0:1, 0:1], min_val=0, max_val=P)
            with dve.If(again > 0):
                with dve.Fori(0, B) as b:
                    dve.wait_ge(g_loaded, 16 * (1 + Q * HALVES) * (b + 1))
                    round_coarse(0, g_coarse)
                    dve.wait_ge(g_rest_made, b + 1)
                    round_middle(0, g_middle)
                    for r in range(R):
                        for hf in range(HALVES):
                            k = HALVES * r + hf
                            if k >= 2:
                                dve.wait_ge(g_transposed, HALVES * R * b + k - 1)
                                nc.vector.memset(scratch[:, :], 0.0)
                            nc.vector.tensor_scalar(mask[:, hf].rearrange("p g m -> p (g m)"),
                                                    adj_sb[:, hf].rearrange("p g m -> p (g m)"),
                                                    float(r + 1), None, ALU.is_equal, saturate=False).then_inc(g_masked, 1)
                            dve.wait_ge(g_masked, HALVES * R * b + k + 1)
                            if k >= 2:
                                dve.wait_ge(g_multiplied, HALVES * R * b + k - 1)
                            transpose_blocks(mask[:, hf], maskT[:, hf]).then_inc(g_transposed, 1)
                    dve.wait_ge(g_projected, b + 1)
                    dve.wait_ge(g_split, 2 * (b + 1))
                    add_and_measure(dve, 0, g_added, b + 1, g_statistics)
                    dve.wait_ge(g_scaled, b + 1)
                    normalize(0, g_normed)
            dve.end_ifs()

        @block.tensor
        def _(pe):
            def step(u, slot):
                b = 2 * u + slot
                for hf in range(HALVES):
                    c = HALVES * b + hf
                    pe.wait_ge(x_split, b + 1)
                    pe.wait_ge(transposed, PIECES * (c + 1))
                    if reached(c, 4):
                        pe.wait_ge(h_copied, c - 3)
                    neighbour_products(hf, HALVES * slot + hf, slot).then_inc(multiplied, 1)
                    if hf == 0 and reached(b, 1):
                        finish(b - 1, 1 - slot)

            def finish(b, slot):
                pe.wait_ge(h_copied, HALVES * (b + 1))
                if reached(b, 2):
                    pe.wait_ge(added, b - 1)
                project(lambda r: h_sb[:, slot], slot, 1).then_inc(projected, 1)

            pe.wait_ge(const_loaded, 32)
            over_batches(pe, step)
            finish(B - 1, 1)
            pe.wait_ge(flag_step, 3)
            pe.wait_ge(h_copied, CHUNKS)
            nc.tensor.matmul(h_ps[0:1, 0, 0:1], above[:, 1:2], ones[:, 0:1], start=True, stop=True).then_inc(flag_counted, 1)

            pe.wait_ge(flag_ready, 1)
            again = pe.value_load(flag[0:1, 0:1], min_val=0, max_val=P)
            with pe.If(again > 0):
                with pe.Fori(0, B) as b:
                    with pe.Fori(0, R) as r:
                        for hf in range(HALVES):
                            pe.wait_ge(g_split, 2 * (b + 1))
                            pe.wait_ge(g_transposed, HALVES * R * b + HALVES * r + hf + 1)
                            neighbour_products(hf, hf, 0).then_inc(g_multiplied, 1)
                            pe.wait_ge(g_h_copied, HALVES * R * b + HALVES * r + hf + 1)
                            pe.wait_ge(flag_ready, 1)
                    project(lambda r: h_all[:, r], 0, R).then_inc(g_projected, 1)
            pe.end_ifs()


_INS = ['x', 'adj', 'L0_gnn_weight', 'L0_gnn_bias']


def kernel(**inputs):
    import numpy as _np
    import concourse.bacc as _bacc
    from concourse import mybir as _mybir
    from concourse.bass_utils import run_bass_kernel_spmd as _run

    nc = _bacc.Bacc("TRN2", target_bir_lowering=False, num_devices=1)
    arrays, args = {}, []
    for name in _INS:
        a = _np.ascontiguousarray(inputs[name])
        arrays[f"in_{name}_dram"] = a
        args.append(nc.dram_tensor(f"in_{name}_dram", a.shape, _mybir.dt.from_np(a.dtype), kind="ExternalInput").ap())
    x = inputs['x']
    out = nc.dram_tensor("out_0_dram", x.shape, _mybir.dt.from_np(_np.dtype(x.dtype)), kind="ExternalOutput").ap()
    relational_layer(nc, *args, out)
    r = _run(nc, [arrays], core_ids=[0])
    return r.results[0]["out_0_dram"]
```

```python
import concourse.bass as bass
from concourse import mybir
from contextlib import ExitStack


Q = 4
LANES = 32
WORD = 4
CH = 4
PARTS = 3
ONE_BITS = 0x38
OTHER_BITS = 0xFFFFFFFF ^ (ONE_BITS * 0x01010101)


def relational_layer(nc, x, adj, weight, bias, out):
    fp32, bf16, fp8 = mybir.dt.float32, mybir.dt.bfloat16, mybir.dt.float8e4
    i32, u32 = mybir.dt.int32, mybir.dt.uint32
    ALU, ACT, AX = mybir.AluOpType, mybir.ActivationFunctionType, mybir.AxisListType

    B, N, D = x.shape
    R = weight.shape[0]
    P = Q * LANES
    MQ = N // Q
    J = MQ // (WORD * LANES)
    TILES = J * WORD
    ROWS = N // CH
    G = ROWS // LANES
    CHUNKS = CH * B
    NADJ = 2 * CH
    LEAD = NADJ - 2
    NMASK = 4
    NBANK = 4
    BANK = 512
    EPS = 1e-5
    LAST = B - 1
    PROJECT_AFTER = 0

    x_p = x.rearrange("b (p t) d -> b p (t d)", p=P)
    out_p = out.rearrange("b (p t) d -> b p (t d)", p=P)
    x_rows = x[B - 1].rearrange("(t p) d -> p t d", p=P)
    out_rows = out[B - 1].rearrange("(t p) d -> p t d", p=P)
    adj_q = adj.rearrange("b (c g i) (q m) -> b c q i g m", c=CH, i=LANES, q=Q)

    ctx = ExitStack()
    with ctx:
        def sb(name, shape, dt):
            return ctx.enter_context(nc.sbuf_tensor(name, shape, dt))

        def pb(name, shape, dt):
            return ctx.enter_context(nc.psum_tensor(name, shape, dt))

        def sem(name):
            return ctx.enter_context(nc.semaphore(name))

        adj_sb = sb("adj_sb", [P, NADJ, G, MQ], i32)
        mask = sb("mask", [P, NMASK, G, MQ], fp8)
        maskT = sb("maskT", [P, NMASK, G, J, LANES, WORD], fp8)
        x_sb = sb("x_sb", [P, 2, TILES, D], fp32)
        x_rest = sb("x_rest", [P, TILES, D], fp32)
        x_part = sb("x_part", [P, 2, PARTS, TILES, D], bf16)
        x_bias = sb("x_bias", [P, 2, TILES, D], fp32)
        h_sb = sb("h_sb", [P, 2, TILES, P], fp32)
        h_all = sb("h_all", [P, R, TILES, P], fp32)
        w_sb = sb("w_sb", [P, R, D], fp32)
        bias_sb = sb("bias_sb", [P, D], fp32)
        total = sb("total", [P, 3, TILES, D], fp32)
        stats = sb("stats", [P, 2, TILES, 6], fp32)
        small = sb("small", [P, 7, TILES], fp32)
        power = sb("power", [P, TILES], fp32)
        mean_var = sb("mean_var", [P, TILES, 2], fp32)
        minus_mean = sb("minus_mean", [P, TILES // CH], fp32)
        last_var = sb("last_var", [P, TILES], fp32)
        scale = sb("scale", [P, 2, TILES], fp32)
        shift = sb("shift", [P, 2, TILES], fp32)
        out_sb = sb("out_sb", [P, B, TILES, D], fp32)
        seen = sb("seen", [P, G * MQ // WORD], u32)
        above = sb("above", [P, 2], fp32)
        scratch = sb("scratch", [P, 1], fp32)
        ones = sb("ones", [P, 1], fp32)
        act_filled = sb("act_filled", [P, NMASK], fp32)
        flag = sb("flag", [1, 1], i32)

        h_ps = pb("h_ps", [P, NBANK, BANK], fp32)
        y_ps = pb("y_ps", [P, 2, TILES, D], fp32)

        weights_loaded = sem("weights_loaded")
        bias_loaded = sem("bias_loaded")
        const_set = sem("const_set")
        x_loaded = [sem(f"x_loaded{s}") for s in range(2)]
        adj_loaded = [sem(f"adj_loaded{s}") for s in range(NADJ)]
        masked = sem("masked")
        collected = sem("collected")
        transposed = sem("transposed")
        coarse = sem("coarse")
        rest_made = sem("rest_made")
        middle = sem("middle")
        x_split = sem("x_split")
        biased = sem("biased")
        multiplied = sem("multiplied")
        h_copied = sem("h_copied")
        projected = sem("projected")
        added = sem("added")
        measured = sem("measured")
        scaled = sem("scaled")
        scale_step = sem("scale_step")
        normed = sem("normed")
        aggregated = sem("aggregated")
        last_var_ready = sem("last_var_ready")
        last_scale_ready = sem("last_scale_ready")
        act_normed = sem("act_normed")
        stored = sem("stored")
        flag_step = sem("flag_step")
        flag_counted = sem("flag_counted")
        flag_ready = sem("flag_ready")
        g_loaded = sem("g_loaded")
        g_coarse = sem("g_coarse")
        g_rest_made = sem("g_rest_made")
        g_middle = sem("g_middle")
        g_split = sem("g_split")
        g_masked = sem("g_masked")
        g_transposed = sem("g_transposed")
        g_multiplied = sem("g_multiplied")
        g_h_copied = sem("g_h_copied")
        g_projected = sem("g_projected")
        g_added = sem("g_added")
        g_measured = sem("g_measured")
        g_scaled = sem("g_scaled")
        g_scale_step = sem("g_scale_step")
        g_normed = sem("g_normed")
        g_stored = sem("g_stored")

        ALL = slice(0, TILES)
        QUARTER = [slice(ch * TILES // CH, (ch + 1) * TILES // CH) for ch in range(CH)]
        HALF = [slice(0, TILES // 2), slice(TILES // 2, TILES)]

        def flat(tiles):
            return tiles.rearrange("p t d -> p (t d)")

        def load_adj(eng, b, ch, slot, quadrants, done):
            for q in quadrants:
                eng.dma_start(adj_sb[q * LANES:(q + 1) * LANES, slot], adj_q[b, ch, q]).then_inc(done, 16)

        def load_x(eng, b, slot, done):
            eng.dma_start(flat(x_sb[:, slot]), x_p[b]).then_inc(done, 16)

        def store(eng, b, place, tiles, done):
            eng.dma_start(out_p[b][:, tiles.start * D:tiles.stop * D], flat(out_sb[:, place, tiles])).then_inc(done, 16)

        def round_coarse(slot, done):
            nc.vector.tensor_copy(flat(x_part[:, slot, 0]), flat(x_sb[:, slot])).then_inc(done, 1)

        def take_rest(eng, slot, done):
            eng.tensor_tensor(flat(x_rest), flat(x_sb[:, slot]), flat(x_part[:, slot, 0]), ALU.subtract).then_inc(done, 1)

        def round_middle(slot, done):
            nc.vector.tensor_copy(flat(x_part[:, slot, 1]), flat(x_rest)).then_inc(done, 1)

        def take_fine(eng, slot, done):
            eng.tensor_tensor(flat(x_part[:, slot, 2]), flat(x_rest), flat(x_part[:, slot, 1]),
                              ALU.subtract).then_inc(done, 1)

        def add_bias(x_slot, slot, done):
            nc.gpsimd.tensor_tensor(x_bias[:, slot], x_sb[:, x_slot],
                                    bias_sb[:, :].unsqueeze(1).to_broadcast([P, TILES, D]), ALU.add).then_inc(done, 1)

        def row_scales(pool, slot, step, base, done):
            st = stats[:, slot]
            m0, m1, s0, s1 = st[:, :, 1], st[:, :, 4], st[:, :, 2], st[:, :, 5]
            mean2, diff, devs, diff_sq, within_4, var_4, half_scale = (small[:, n, :] for n in range(7))
            nc.gpsimd.tensor_tensor(mean2, m0, m1, ALU.add)
            nc.gpsimd.tensor_tensor(diff, m0, m1, ALU.subtract)
            nc.gpsimd.tensor_tensor(devs, s0, s1, ALU.add).then_inc(step, 1)
            pool.wait_ge(step, base + 1)
            nc.gpsimd.tensor_tensor(diff_sq, diff, diff, ALU.mult)
            nc.gpsimd.tensor_scalar(within_4, devs, 4.0 / D, 4.0 * EPS, ALU.mult, ALU.add).then_inc(step, 1)
            pool.wait_ge(step, base + 2)
            nc.gpsimd.tensor_tensor(var_4, diff_sq, within_4, ALU.add).then_inc(step, 1)
            pool.wait_ge(step, base + 3)
            nc.gpsimd.tensor_tensor(half_scale, var_4, power[:, :], ALU.pow)
            nc.gpsimd.tensor_scalar(mean2, mean2, -1.0, 0.0, ALU.mult, ALU.add).then_inc(step, 1)
            pool.wait_ge(step, base + 4)
            nc.gpsimd.tensor_tensor(scale[:, slot, :], half_scale, half_scale, ALU.add)
            nc.gpsimd.tensor_tensor(shift[:, slot, :], mean2, half_scale, ALU.mult).then_inc(done, 1)

        def last_variances(dve, tiles, half):
            dve.wait_ge(measured, LAST + (half + 1) * CH // 2)
            for t in range(tiles.start, tiles.stop):
                last = nc.vector.bn_aggr(mean_var[:, t, :], stats[:, 1, t, :])
            last.then_inc(aggregated, 1)
            dve.wait_ge(aggregated, half + 1)
            if half == 1:
                nc.vector.tensor_scalar(minus_mean[:, :], mean_var[:, QUARTER[2], 0], -1.0, None, ALU.mult)
            nc.vector.tensor_scalar(last_var[:, tiles], mean_var[:, tiles, 1], EPS, None, ALU.add).then_inc(last_var_ready, 1)

        def last_scales(pool, tiles, half):
            pool.wait_ge(last_var_ready, half + 1)
            if half == 0:
                pool.wait_ge(act_normed, 1)
            nc.gpsimd.tensor_tensor(scale[:, 1, tiles], last_var[:, tiles], power[:, tiles], ALU.pow).then_inc(last_scale_ready, 1)
            if half == 1:
                pool.wait_ge(last_scale_ready, 2)
                nc.gpsimd.tensor_tensor(shift[:, 1, QUARTER[2]], minus_mean[:, :], scale[:, 1, QUARTER[2]],
                                        ALU.mult).then_inc(scaled, 1)

        def last_y(ch):
            first = ch % 2 * TILES // 2
            return y_ps[:, 1 - ch // 2, first:first + TILES // CH]

        def sum_up(y, slot, place, tiles, done):
            nc.vector.tensor_tensor(total[:, place, tiles], y, x_bias[:, slot, tiles],
                                    ALU.add).then_inc(done, 1)

        def measure_rows(slot, place, tiles, done):
            for t in range(tiles.start, tiles.stop):
                last = nc.vector.bn_stats(stats[:, slot, t, :], total[:, place, t, :])
            if done:
                last.then_inc(done, 1)

        def normalize(b, slot, tiles, done):
            for t in range(tiles.start, tiles.stop):
                last = nc.vector.tensor_scalar(out_sb[:, b, t, :], total[:, slot, t, :], scale[:, slot, t:t + 1],
                                               shift[:, slot, t:t + 1], ALU.mult, ALU.add)
            if done:
                last.then_inc(done, 1)

        def words(values):
            return values.rearrange("p g m -> p (g m)").bitcast(u32)

        def transpose_blocks(slot, done):
            blocks = words(mask[:, slot]).rearrange("p (g k j) -> p g j k", k=LANES, j=J)
            nc.vector.transpose(maskT[:, slot].rearrange("p g j i e -> p (g j i e)").bitcast(u32), blocks).then_inc(done, 1)

        def neighbour_products(mask_slot, bank, slot, done):
            h = h_ps[:, bank, 0:ROWS]
            nc.tensor.matmul(h[:, 0:1], x_part[:, slot, 0, 0, :], x_part[:, slot, 0, 0, 0:1], start=True, stop=True)
            for t in range(TILES):
                for part in range(PARTS):
                    step = t * PARTS + part
                    last = nc.tensor.matmul(h, x_part[:, slot, part, t, :], maskT[:, mask_slot, :, t // WORD, :, t % WORD],
                                            start=(step == 0), stop=(step == TILES * PARTS - 1))
            last.then_inc(done, 1)

        def copy_chunk(h, ch, bank, done):
            places = slice(ch * P // CH, (ch + 1) * P // CH)
            nc.scalar.copy(h[:, :, places].rearrange("d t p -> d p t"),
                           h_ps[:, bank, 0:ROWS].rearrange("d (p t) -> d p t", t=TILES)).then_inc(done, 1)

        def project(h_of, y, relations, tiles, done):
            for t in range(tiles.start, tiles.stop):
                for r in range(relations):
                    last = nc.tensor.matmul(y[:, t - tiles.start, :], h_of(r)[:, t], w_sb[:, r, :],
                                            start=(r == 0), stop=(r == relations - 1))
            last.then_inc(done, 1)

        def over_batches(eng, step):
            def pair(u):
                for slot in range(2):
                    step(u, slot)
            pair(0)
            with eng.Fori(1, B // 2 - 1) as u:
                pair(u)
            pair(B // 2 - 1)

        def reached(n, least):
            return n >= least if type(n) is int else True

        def within(n, end):
            return n < end if type(n) is int else True

        def load_ahead(sp, u, slot, ch):
            b = 2 * u + slot
            c = CH * b + ch
            if not reached(c, 2) or not within(c + LEAD, CHUNKS):
                return
            sp.wait_ge(masked, c - 1)
            ahead = ch + LEAD
            place = (CH * slot + ahead) % NADJ
            load_adj(sp, b + ahead // CH, ahead % CH, place, range(Q), adj_loaded[place])

        block = ctx.enter_context(nc.Block())

        @block.sync
        def _(sp):
            def load_x_after(b, slot):
                sp.wait_ge(rest_made, b + 1)
                sp.wait_ge(biased, b + 1)
                load_x(sp, b + 2, slot, x_loaded[slot])

            load_x(sp, 0, 0, x_loaded[0])
            for c in range(NADJ):
                if c == LEAD:
                    load_x_after(0, 0)
                load_adj(sp, c // CH, c % CH, c, (0, 1) if c == 0 else range(Q), adj_loaded[c])
                if c == 1:
                    sp.dma_start(bias_sb[:, :], bias.unsqueeze(0).to_broadcast([P, D])).then_inc(bias_loaded, 16)
                    load_x(sp, 1, 1, x_loaded[1])
                if c == 3:
                    sp.dma_start(w_sb[:, 0, :], weight[0]).then_inc(weights_loaded, 16)

            def step(u, slot):
                b = 2 * u + slot
                if reached(b, 1) and within(b + 2, B):
                    load_x_after(b, slot)
                for ch in range(CH):
                    load_ahead(sp, u, slot, ch)

            over_batches(sp, step)
            sp.wait_ge(rest_made, LAST)
            sp.wait_ge(biased, LAST)
            sp.dma_start(x_sb[:, 0], x_rows).then_inc(x_loaded[0], 16)
            for b in range(LAST - 2):
                sp.wait_ge(normed, b + 1)
                store(sp, b, b, ALL, stored)
            sp.wait_ge(act_normed, 1)
            store(sp, LAST - 2, LAST - 2, ALL, stored)
            for half in range(2):
                sp.wait_ge(act_normed, 2 + half)
                store(sp, LAST - 1, LAST - 1, HALF[half], stored)
            for tiles, by, count in ((HALF[0], normed, LAST - 1), (QUARTER[2], act_normed, 4), (QUARTER[3], normed, LAST)):
                sp.wait_ge(by, count)
                sp.dma_start(out_rows[:, tiles], out_sb[:, LAST, tiles]).then_inc(stored, 16)
            sp.wait_ge(flag_ready, 1)
            again = sp.value_load(flag[0:1, 0:1], min_val=0, max_val=P)
            sp.wait_ge(stored, 16 * (LAST + 4))
            with sp.If(again > 0):
                sp.dma_start(w_sb[:, 1:R, :], weight[1:R].rearrange("r d o -> d r o")).then_inc(weights_loaded, 16)
                sp.sem_inc(g_stored, 16)
                with sp.Fori(0, B) as b:
                    sp.wait_ge(g_stored, 16 * (b + 1))
                    load_x(sp, b, 0, g_loaded)
                    for ch in range(CH):
                        load_adj(sp, b, ch, ch, range(Q), g_loaded)
                    sp.wait_ge(g_normed, b + 1)
                    store(sp, b, 0, ALL, g_stored)
                sp.wait_ge(g_stored, 16 * (B + 1))
            sp.end_ifs()

        @block.gpsimd
        def _(pool):
            nc.gpsimd.memset(power[:, :], -0.5)
            nc.gpsimd.memset(ones[:, :], 1.0).then_inc(const_set, 1)
            pool.wait_ge(const_set, 1)

            def rest(b, slot):
                pool.wait_ge(coarse, b + 1)
                if reached(b, 1):
                    pool.wait_ge(x_split, b)
                take_rest(nc.gpsimd, slot, rest_made)

            def fine(b, slot):
                pool.wait_ge(middle, b + 1)
                take_fine(nc.gpsimd, slot, x_split)
                if not within(b, LAST):
                    return
                if reached(b, 2):
                    pool.wait_ge(added, b - 1)
                add_bias(slot, slot, biased)

            def scales(b, slot):
                pool.wait_ge(measured, b + 1)
                row_scales(pool, slot, scale_step, 4 * b, scaled)

            def step(u, slot):
                b = 2 * u + slot
                if reached(b, 2):
                    scales(b - 2, slot)
                if within(b + 1, B):
                    rest(b + 1, 1 - slot)
                    fine(b + 1, 1 - slot)

            pool.wait_ge(x_loaded[0], 16)
            pool.wait_ge(bias_loaded, 16)
            add_bias(0, 0, biased)
            over_batches(pool, step)
            pool.wait_ge(x_loaded[0], 16 * (B // 2 + 1))
            pool.wait_ge(added, LAST - 1)
            add_bias(0, 1, biased)
            pool.wait_ge(scaled, LAST - 1)
            scales(LAST - 1, 0)
            for half in range(2):
                last_scales(pool, HALF[half], half)

            pool.wait_ge(flag_ready, 1)
            again = pool.value_load(flag[0:1, 0:1], min_val=0, max_val=P)
            with pool.If(again > 0):
                with pool.Fori(0, B) as b:
                    pool.wait_ge(g_coarse, b + 1)
                    take_rest(nc.gpsimd, 0, g_rest_made)
                    add_bias(0, 0, g_split)
                    pool.wait_ge(g_middle, b + 1)
                    take_fine(nc.gpsimd, 0, g_split)
                    pool.wait_ge(g_measured, b + 1)
                    row_scales(pool, 0, g_scale_step, 4 * b, g_scaled)
            pool.end_ifs()

        @block.scalar
        def _(act):
            load_adj(act, 0, 0, 0, (2, 3), adj_loaded[0])
            act.wait_ge(const_set, 1)
            nc.scalar.copy(act_filled[:, 0:1], ones[:, :])

            def copy_h(b, slot, ch):
                act.wait_ge(multiplied, CH * b + ch + 1)
                if reached(b, 2):
                    act.wait_ge(projected, 2 * (b - 1))
                if within(b, LAST):
                    copy_chunk(h_sb[:, slot], ch, ch % NBANK, h_copied)
                else:
                    nc.scalar.copy(h_sb[:, slot, QUARTER[ch]].rearrange("d t p -> d (t p)"),
                                   h_ps[:, ch % NBANK, 0:ROWS]).then_inc(h_copied, 1)

            def step(u, slot):
                b = 2 * u + slot
                for ch in range(CH):
                    c = CH * b + ch
                    place = CH * slot + ch
                    act.wait_ge(adj_loaded[place], 16 * Q * (u + 1))
                    if reached(c, NMASK):
                        act.wait_ge(transposed, c - NMASK + 1)
                        act.wait_ge(collected, c - NMASK + 2)
                    if reached(c, 1):
                        nc.scalar.copy(act_filled[:, ch:ch + 1], ones[:, :])
                    nc.scalar.activation(mask[:, ch % NMASK].rearrange("p g m -> p (g m)"),
                                         adj_sb[:, place].rearrange("p g m -> p (g m)"), ACT.Copy,
                                         saturate=False).then_inc(masked, 1)
                    if ch >= 2:
                        copy_h(b, slot, ch - 2)
                    elif reached(b, 1):
                        copy_h(b - 1, 1 - slot, CH + ch - 2)

            over_batches(act, step)
            def finish(b, slot, place, tiles, scales_made):
                act.wait_ge(scaled, scales_made)
                for t in range(tiles.start, tiles.stop):
                    last = nc.scalar.activation(out_sb[:, b, t, :], total[:, place, t, :], ACT.Identity,
                                                bias=shift[:, slot, t:t + 1], scale=scale[:, slot, t:t + 1])
                last.then_inc(act_normed, 1)

            finish(LAST - 2, 1, 1, ALL, LAST - 1)
            copy_h(LAST, 1, CH - 2)
            copy_h(LAST, 1, CH - 1)
            finish(LAST - 1, 0, 0, HALF[0], LAST)
            finish(LAST - 1, 0, 0, HALF[1], LAST)
            finish(LAST, 1, 2, QUARTER[2], LAST + 1)

            act.wait_ge(flag_ready, 1)
            again = act.value_load(flag[0:1, 0:1], min_val=0, max_val=P)
            with act.If(again > 0):
                with act.Fori(0, B) as b:
                    with act.Fori(0, R) as r:
                        for ch in range(CH):
                            act.wait_ge(g_multiplied, CH * R * b + CH * r + ch + 1)
                            copy_chunk(h_all[:, r], ch, ch % NBANK, g_h_copied)
            act.end_ifs()

        @block.vector
        def _(dve):
            nc.vector.memset(seen[:, :], 0).then_inc(collected, 1)

            def coarse_part(b, slot, u):
                dve.wait_ge(x_loaded[slot], 16 * (u + 1))
                if reached(b, 2):
                    dve.wait_ge(multiplied, CH * (b - 1))
                round_coarse(slot, coarse)

            def middle_part(b, slot):
                dve.wait_ge(rest_made, b + 1)
                round_middle(slot, middle)

            def add(b, slot):
                dve.wait_ge(projected, 2 * (b + 1))
                dve.wait_ge(biased, b + 1)
                if reached(b, 2):
                    dve.wait_ge(normed, b - 1)
                sum_up(y_ps[:, slot], slot, slot, ALL, added)

            def measure(b, slot, half):
                if half == 0:
                    dve.wait_ge(added, b + 1)
                measure_rows(slot, slot, HALF[half], measured if half == 1 else None)

            def finish(b, slot, half):
                if half == 0:
                    dve.wait_ge(scaled, b + 1)
                normalize(b, slot, HALF[half], normed if half == 1 else None)

            def step(u, slot):
                b = 2 * u + slot
                for ch in range(CH):
                    c = CH * b + ch
                    dve.wait_ge(masked, c + 1)
                    if reached(c, NMASK):
                        dve.wait_ge(multiplied, c - NMASK + 1)
                    transpose_blocks(ch % NMASK, transposed)
                    dve.wait_ge(collected, c + 1)
                    nc.vector.tensor_tensor(seen[:, :], seen[:, :], words(mask[:, ch % NMASK]),
                                            ALU.bitwise_or).then_inc(collected, 1)
                    if ch == 0 and reached(b, 2):
                        if not within(b, LAST):
                            measure(b - 2, slot, 0)
                        measure(b - 2, slot, 1)
                    if ch == 1 and within(b + 1, B):
                        coarse_part(b + 1, 1 - slot, u + slot)
                    if ch == 2 and within(b + 1, B):
                        middle_part(b + 1, 1 - slot)
                    if ch in (1, 2) and reached(b, 2) and within(b, LAST):
                        finish(b - 2, slot, ch - 1)
                    if ch == (3 if within(b, LAST) else 2) and reached(b, 1):
                        add(b - 1, 1 - slot)
                        if type(b) is not int or b != LAST - 1:
                            measure(b - 1, 1 - slot, 0)

            def find_others():
                dve.wait_ge(collected, CHUNKS + 1)
                nc.vector.tensor_scalar(seen[:, :], seen[:, :], OTHER_BITS, None, ALU.bitwise_and).then_inc(flag_step, 1)
                dve.wait_ge(flag_step, 1)
                nc.vector.reduce_max(above[:, 0:1], seen[:, :], AX.X).then_inc(flag_step, 1)
                dve.wait_ge(flag_step, 2)
                nc.vector.tensor_scalar(above[:, 1:2], above[:, 0:1], 0.0, None, ALU.is_gt).then_inc(flag_step, 1)

            coarse_part(0, 0, 0)
            dve.wait_ge(coarse, 1)
            take_rest(nc.vector, 0, rest_made)
            middle_part(0, 0)
            dve.wait_ge(middle, 1)
            take_fine(nc.vector, 0, x_split)
            over_batches(dve, step)
            measure(LAST - 1, 0, 1)
            dve.wait_ge(biased, B)
            for ch in range(CH):
                tiles = QUARTER[ch]
                dve.wait_ge(projected, 2 * LAST + ch + 1)
                sum_up(last_y(ch), 1, 2, tiles, added)
                dve.wait_ge(added, LAST + ch + 1)
                measure_rows(1, 2, tiles, measured)
                if ch == CH // 2 - 1:
                    last_variances(dve, HALF[0], 0)
                    find_others()
            last_variances(dve, HALF[1], 1)
            for half, tiles in ((0, HALF[0]), (1, QUARTER[3])):
                dve.wait_ge(last_scale_ready, half + 1)
                for t in range(tiles.start, tiles.stop):
                    last = nc.vector.tensor_scalar(out_sb[:, LAST, t, :], total[:, 2, t, :], mean_var[:, t, 0:1],
                                                   scale[:, 1, t:t + 1], ALU.subtract, ALU.mult)
                last.then_inc(normed, 1)
            dve.wait_ge(flag_counted, 1)
            nc.vector.tensor_copy(flag[:, :], h_ps[0:1, 0, 0:1]).then_inc(flag_ready, 1)

            dve.wait_ge(flag_ready, 1)
            again = dve.value_load(flag[0:1, 0:1], min_val=0, max_val=P)
            with dve.If(again > 0):
                with dve.Fori(0, B) as b:
                    dve.wait_ge(g_loaded, 16 * (1 + Q * CH) * (b + 1))
                    round_coarse(0, g_coarse)
                    dve.wait_ge(g_rest_made, b + 1)
                    round_middle(0, g_middle)
                    for r in range(R):
                        for ch in range(CH):
                            k = CH * R * b + CH * r + ch
                            slot = ch % NMASK
                            if r > 0:
                                dve.wait_ge(g_transposed, k - NMASK + 1)
                                nc.vector.memset(scratch[:, :], 0.0)
                            nc.vector.tensor_scalar(mask[:, slot].rearrange("p g m -> p (g m)"),
                                                    adj_sb[:, ch].rearrange("p g m -> p (g m)"),
                                                    float(r + 1), None, ALU.is_equal, saturate=False).then_inc(g_masked, 1)
                            dve.wait_ge(g_masked, k + 1)
                            if r > 0:
                                dve.wait_ge(g_multiplied, k - NMASK + 1)
                            transpose_blocks(slot, g_transposed)
                    dve.wait_ge(g_projected, b + 1)
                    dve.wait_ge(g_split, 2 * (b + 1))
                    sum_up(y_ps[:, 0], 0, 0, ALL, g_added)
                    dve.wait_ge(g_added, b + 1)
                    measure_rows(0, 0, ALL, g_measured)
                    dve.wait_ge(g_scaled, b + 1)
                    normalize(0, 0, ALL, g_normed)
            dve.end_ifs()

        @block.tensor
        def _(pe):
            def finish(b, slot):
                pe.wait_ge(h_copied, CH * (b + 1))
                if reached(b, 2):
                    pe.wait_ge(added, b - 1)
                if not reached(b, 1):
                    pe.wait_ge(weights_loaded, 16)
                for half in range(2):
                    project(lambda r: h_sb[:, slot], y_ps[:, slot, HALF[half]], 1, HALF[half], projected)

            def finish_tiles(ch):
                pe.wait_ge(h_copied, CH * LAST + ch + 1)
                pe.wait_ge(added, LAST - 1 + ch // 2)
                project(lambda r: h_sb[:, 1], last_y(ch), 1, QUARTER[ch], projected)

            def step(u, slot):
                b = 2 * u + slot
                for ch in range(CH):
                    c = CH * b + ch
                    pe.wait_ge(x_split, b + 1)
                    pe.wait_ge(transposed, c + 1)
                    if reached(c, NBANK):
                        pe.wait_ge(h_copied, c - NBANK + 1)
                    neighbour_products(ch % NMASK, ch % NBANK, slot, multiplied)
                    if ch == PROJECT_AFTER and reached(b, 1):
                        finish(b - 1, 1 - slot)
                    if ch in (1, 2) and not within(b, LAST):
                        finish_tiles(ch - 1)

            over_batches(pe, step)
            finish_tiles(2)
            finish_tiles(3)
            pe.wait_ge(flag_step, 3)
            nc.tensor.matmul(h_ps[0:1, 0, 0:1], above[:, 1:2], ones[:, 0:1], start=True, stop=True).then_inc(flag_counted, 1)

            pe.wait_ge(flag_ready, 1)
            again = pe.value_load(flag[0:1, 0:1], min_val=0, max_val=P)
            with pe.If(again > 0):
                pe.wait_ge(weights_loaded, 32)
                with pe.Fori(0, B) as b:
                    with pe.Fori(0, R) as r:
                        for ch in range(CH):
                            pe.wait_ge(g_split, 2 * (b + 1))
                            pe.wait_ge(g_transposed, CH * R * b + CH * r + ch + 1)
                            neighbour_products(ch % NMASK, ch % NBANK, 0, g_multiplied)
                            pe.wait_ge(g_h_copied, CH * R * b + CH * r + ch + 1)
                            pe.wait_ge(flag_ready, 1)
                    project(lambda r: h_all[:, r], y_ps[:, 0], R, ALL, g_projected)
            pe.end_ifs()


_INS = ['x', 'adj', 'L0_gnn_weight', 'L0_gnn_bias']


def kernel(**inputs):
    import numpy as _np
    import concourse.bacc as _bacc
    from concourse import mybir as _mybir
    from concourse.bass_utils import run_bass_kernel_spmd as _run

    nc = _bacc.Bacc("TRN2", target_bir_lowering=False, num_devices=1)
    arrays, args = {}, []
    for name in _INS:
        a = _np.ascontiguousarray(inputs[name])
        arrays[f"in_{name}_dram"] = a
        args.append(nc.dram_tensor(f"in_{name}_dram", a.shape, _mybir.dt.from_np(a.dtype), kind="ExternalInput").ap())
    x = inputs['x']
    out = nc.dram_tensor("out_0_dram", x.shape, _mybir.dt.from_np(_np.dtype(x.dtype)), kind="ExternalOutput").ap()
    relational_layer(nc, *args, out)
    r = _run(nc, [arrays], core_ids=[0])
    return r.results[0]["out_0_dram"]
```
